# Optimizing a Trainium2 kernel written in Bass

```python
import numpy as np
import jax
import jax.numpy as jnp

def _softmax(x, axis=-1):
    return jax.nn.softmax(x, axis=axis)

def _gelu(x):
    return jax.nn.gelu(x, approximate=True)

def _silu(x):
    return jax.nn.silu(x)

def _sigmoid(x):
    return jax.nn.sigmoid(x)

def _layernorm(x, axis=-1, eps=1e-05):
    m = jnp.mean(x, axis=axis, keepdims=True)
    v = jnp.var(x, axis=axis, keepdims=True)
    return (x - m) / jnp.sqrt(v + eps)

def _scatter_add(tgt, idx, src, axis=0):
    return tgt.at[idx].add(src)

def _segment_sum(src, seg, n):
    return jax.ops.segment_sum(src, seg, n)
kernel_name = 'mk_rec_standalone_d1_rec_r8_c63112'

def setup_inputs(seed: int=0):
    np.random.seed(seed)
    _w = jnp.asarray

    def _rec_inputs():
        import jax
        import jax.numpy as jnp
        _rk = jax.random.key(seed)
        r_dense_x = 8.7408e-05 + 1.0001 * jax.random.normal(jax.random.fold_in(_rk, 1), (512, 13), jnp.float32)
        r_sparse_x = jnp.stack([jax.random.randint(jax.random.fold_in(jax.random.fold_in(_rk, 2), 0), (512,), 2, 12500, jnp.int32), jax.random.randint(jax.random.fold_in(jax.random.fold_in(_rk, 2), 1), (512,), 1, 99999, jnp.int32), jax.random.randint(jax.random.fold_in(jax.random.fold_in(_rk, 2), 2), (512,), 0, 12500, jnp.int32), jax.random.randint(jax.random.fold_in(jax.random.fold_in(_rk, 2), 3), (512,), 0, 12500, jnp.int32), jax.random.randint(jax.random.fold_in(jax.random.fold_in(_rk, 2), 4), (512,), 10, 99997, jnp.int32), jax.random.randint(jax.random.fold_in(jax.random.fold_in(_rk, 2), 5), (512,), 0, 99993, jnp.int32), jax.random.randint(jax.random.fold_in(jax.random.fold_in(_rk, 2), 6), (512,), 2, 99999, jnp.int32), jax.random.randint(jax.random.fold_in(jax.random.fold_in(_rk, 2), 7), (512,), 1, 99995, jnp.int32), jax.random.randint(jax.random.fold_in(jax.random.fold_in(_rk, 2), 8), (512,), 0, 12500, jnp.int32), jax.random.randint(jax.random.fold_in(jax.random.fold_in(_rk, 2), 9), (512,), 2, 99999, jnp.int32), jax.random.randint(jax.random.fold_in(jax.random.fold_in(_rk, 2), 10), (512,), 0, 99999, jnp.int32), jax.random.randint(jax.random.fold_in(jax.random.fold_in(_rk, 2), 11), (512,), 6, 99999, jnp.int32), jax.random.randint(jax.random.fold_in(jax.random.fold_in(_rk, 2), 12), (512,), 0, 99999, jnp.int32), jax.random.randint(jax.random.fold_in(jax.random.fold_in(_rk, 2), 13), (512,), 3, 99996, jnp.int32), jax.random.randint(jax.random.fold_in(jax.random.fold_in(_rk, 2), 14), (512,), 0, 99999, jnp.int32), jax.random.randint(jax.random.fold_in(jax.random.fold_in(_rk, 2), 15), (512,), 3, 99997, jnp.int32), jax.random.randint(jax.random.fold_in(jax.random.fold_in(_rk, 2), 16), (512,), 0, 99999, jnp.int32), jax.random.randint(jax.random.fold_in(jax.random.fold_in(_rk, 2), 17), (512,), 0, 99998, jnp.int32), jax.random.randint(jax.random.fold_in(jax.random.fold_in(_rk, 2), 18), (512,), 10, 99997, jnp.int32), jax.random.randint(jax.random.fold_in(jax.random.fold_in(_rk, 2), 19), (512,), 0, 99999, jnp.int32), jax.random.randint(jax.random.fold_in(jax.random.fold_in(_rk, 2), 20), (512,), 0, 12500, jnp.int32), jax.random.randint(jax.random.fold_in(jax.random.fold_in(_rk, 2), 21), (512,), 1, 12500, jnp.int32), jax.random.randint(jax.random.fold_in(jax.random.fold_in(_rk, 2), 22), (512,), 1, 99997, jnp.int32), jax.random.randint(jax.random.fold_in(jax.random.fold_in(_rk, 2), 23), (512,), 2, 12500, jnp.int32), jax.random.randint(jax.random.fold_in(jax.random.fold_in(_rk, 2), 24), (512,), 1, 12500, jnp.int32), jax.random.randint(jax.random.fold_in(jax.random.fold_in(_rk, 2), 25), (512,), 2, 99995, jnp.int32)], axis=1)
        return (r_dense_x, r_sparse_x)
    r_dense_x, r_sparse_x = _rec_inputs()

    def _L0_rec_setup():
        import jax, jax.numpy as jnp
        import numpy as np
        B = 4096
        NUM_SPARSE = 26
        VOCAB = 12500
        EMB = 128
        DENSE_IN = 13
        N_FIELDS = NUM_SPARSE + 1
        INTER_DIM = N_FIELDS * (N_FIELDS - 1) // 2
        TOP_IN = EMB + INTER_DIM
        key = jax.random.key(seed)
        ks = jax.random.split(key, 12)
        inp = {'dense_x': jax.random.normal(ks[0], (B, DENSE_IN), dtype=jnp.float32), 'sparse_x': jax.random.randint(ks[1], (B, NUM_SPARSE), 0, VOCAB, dtype=jnp.int64), 'emb_tables': jax.random.normal(ks[2], (NUM_SPARSE, VOCAB, EMB), dtype=jnp.float32) * 0.02, 'bw1': jax.random.normal(ks[3], (DENSE_IN, 256), dtype=jnp.float32) * 0.1, 'bb1': jnp.zeros((256,), dtype=jnp.float32), 'bw2': jax.random.normal(ks[4], (256, EMB), dtype=jnp.float32) * 0.05, 'bb2': jnp.zeros((EMB,), dtype=jnp.float32), 'tw1': jax.random.normal(ks[5], (TOP_IN, 128), dtype=jnp.float32) * 0.05, 'tb1': jnp.zeros((128,), dtype=jnp.float32), 'tw2': jax.random.normal(ks[6], (128, 64), dtype=jnp.float32) * 0.1, 'tb2': jnp.zeros((64,), dtype=jnp.float32), 'tw3': jax.random.normal(ks[7], (64, 1), dtype=jnp.float32) * 0.1, 'tb3': jnp.zeros((1,), dtype=jnp.float32)}
        return inp
    _L0_rec_all = _L0_rec_setup()
    _L0_rec_in = {k: v for k, v in _L0_rec_all.items() if k in ('emb_tables', 'bw1', 'bb1', 'bw2', 'bb2', 'tw1', 'tb1', 'tw2', 'tb2', 'tw3', 'tb3')}
    del _L0_rec_all
    return {'r_dense_x': r_dense_x, 'r_sparse_x': r_sparse_x, 'L0_rec_emb_tables': _L0_rec_in['emb_tables'], 'L0_rec_bw1': _L0_rec_in['bw1'], 'L0_rec_bb1': _L0_rec_in['bb1'], 'L0_rec_bw2': _L0_rec_in['bw2'], 'L0_rec_bb2': _L0_rec_in['bb2'], 'L0_rec_tw1': _L0_rec_in['tw1'], 'L0_rec_tb1': _L0_rec_in['tb1'], 'L0_rec_tw2': _L0_rec_in['tw2'], 'L0_rec_tb2': _L0_rec_in['tb2'], 'L0_rec_tw3': _L0_rec_in['tw3'], 'L0_rec_tb3': _L0_rec_in['tb3']}

def reference(r_dense_x, r_sparse_x, L0_rec_emb_tables, L0_rec_bw1, L0_rec_bb1, L0_rec_bw2, L0_rec_bb2, L0_rec_tw1, L0_rec_tb1, L0_rec_tw2, L0_rec_tb2, L0_rec_tw3, L0_rec_tb3):
    import jax
    import jax.numpy as jnp

    def _L0_rec_ref(dense_x, sparse_x, emb_tables, bw1, bb1, bw2, bb2, tw1, tb1, tw2, tb2, tw3, tb3):
        import jax, jax.numpy as jnp
        import numpy as np
        B = 4096
        NUM_SPARSE = 26
        VOCAB = 12500
        EMB = 128
        DENSE_IN = 13
        N_FIELDS = NUM_SPARSE + 1
        INTER_DIM = N_FIELDS * (N_FIELDS - 1) // 2
        TOP_IN = EMB + INTER_DIM
        h = jax.nn.relu(dense_x @ bw1 + bb1)
        x_bottom = jax.nn.relu(h @ bw2 + bb2)
        field_idx = jnp.arange(NUM_SPARSE)[None, :]
        sparse_embs = emb_tables[field_idx, sparse_x]
        combined = jnp.concatenate([x_bottom[:, None, :], sparse_embs], axis=1)
        interactions = jnp.einsum('bfd,bgd->bfg', combined, combined)
        rows, cols = np.triu_indices(N_FIELDS, k=1)
        x_int = interactions[:, rows, cols]
        x_final = jnp.concatenate([x_bottom, x_int], axis=-1)
        t = jax.nn.relu(x_final @ tw1 + tb1)
        t = jax.nn.relu(t @ tw2 + tb2)
        logits = t @ tw3 + tb3
        return jax.nn.sigmoid(logits)
    y = _L0_rec_ref(r_dense_x, r_sparse_x, L0_rec_emb_tables, L0_rec_bw1, L0_rec_bb1, L0_rec_bw2, L0_rec_bb2, L0_rec_tw1, L0_rec_tb1, L0_rec_tw2, L0_rec_tb2, L0_rec_tw3, L0_rec_tb3)
    return y

_drawn_inputs = setup_inputs


def setup_inputs(seed=0):
    import zlib

    import numpy as np

    out = dict(_drawn_inputs(seed))
    spreads = {'L0_rec_bb1': (0.0, 0.8),
     'L0_rec_bb2': (0.0, 0.8),
     'L0_rec_tb1': (0.0, 1.935),
     'L0_rec_tb2': (0.0, 2.0)}
    factors = {'r_dense_x': 5.77,
     'L0_rec_emb_tables': 8.0,
     'L0_rec_bw1': 4.993,
     'L0_rec_bw2': 4.877,
     'L0_rec_tw1': 4.279,
     'L0_rec_tw2': 3.216}
    for name, (base, spread) in spreads.items():
        noise = np.random.default_rng([zlib.crc32(name.encode()), seed]).standard_normal(out[name].shape)
        drawn = base * np.exp(spread * noise) if base else spread * noise
        out[name] = jnp.asarray(drawn.astype(out[name].dtype))
    for name, factor in factors.items():
        out[name] = (out[name] * factor).astype(out[name].dtype)
    return out
```

```python
import concourse.bass as bass
from concourse import mybir
from contextlib import ExitStack
from math import lcm

P = 128
BATCH = 512
SPARSE = 26
VOCAB = 12500
EMB = 128
DENSE = 13
HID = 256
T1, T2 = 128, 64
HH = HID // P

SLOT = 32
QUAD = P // SLOT
GROUP_ROWS = lcm(SPARSE, P)
GROUP_CHUNKS = GROUP_ROWS // P
GROUP = GROUP_ROWS // SPARSE
GROUPS = BATCH // GROUP
ROUNDS = GROUPS // 2

BANK = 512
UNIT_CHUNKS = BANK // P
UNITS = [(c, min(c + UNIT_CHUNKS, GROUP_CHUNKS)) for c in range(0, GROUP_CHUNKS, UNIT_CHUNKS)]

SPLIT = 2
PART = -(-SPARSE // SPLIT)
PAIR_ROWS = SLOT * SPLIT

BATCH_QUADS = 4


def quad_batches():
    out, at = [], 0
    quads = GROUP // QUAD
    for u, (_, c1) in enumerate(UNITS):
        ready = c1 * P // SPARSE // QUAD
        while ready - at >= BATCH_QUADS or (u >= len(UNITS) - 2 and ready > at):
            end = min(at + BATCH_QUADS, ready)
            out.append((u, at, end))
            at = end
    assert at == quads
    return out


BATCHES = quad_batches()


def evacuation_pieces(c0, c1):
    row, end, out = c0 * P, c1 * P, []
    while row < end:
        b, f = divmod(row, SPARSE)
        if f or end - row < SPARSE:
            n = min(SPARSE - f, end - row)
            out.append((row - c0 * P, 1, b, f, n))
            row += n
        else:
            k = (end - row) // SPARSE
            out.append((row - c0 * P, k, b, 0, SPARSE))
            row += k * SPARSE
    return out


IDENT = 0
BW2 = IDENT + P
TW1X = BW2 + HH * EMB
TW2 = TW1X + T1
TW3 = TW2 + T2
BB1 = TW3 + 1
BB2 = BB1 + HH
TB1 = BB2 + 1
TB2 = TB1 + 1
TB3 = TB2 + 1
WEIGHTS = TB3 + 1


def dlrm(nc, index_base, dense_bw1, weights, pair_weights, table, out):
    fp32, i32, u32 = mybir.dt.float32, mybir.dt.int32, mybir.dt.uint32
    ALU = mybir.AluOpType
    ACT = mybir.ActivationFunctionType
    NB, NU = len(BATCHES), len(UNITS)

    ctx = ExitStack()
    with ctx:
        def sb(name, shape, dt=fp32):
            return ctx.enter_context(nc.sbuf_tensor(name, shape, dt))

        def sem(name):
            return ctx.enter_context(nc.semaphore(name))

        banks = [ctx.enter_context(nc.psum_tensor(f"bank{i}", [P, BANK], fp32)) for i in range(8)]
        rows_T = banks[0:2]
        products = banks[2:4]
        top1_ps, top2_ps, logit_ps = banks[4], banks[5], banks[6]

        raw = sb("raw", [P, GROUPS * GROUP_CHUNKS + GROUP_CHUNKS], i32)
        wrap = sb("wrap", [P, GROUP_CHUNKS], i32)
        wrapped = sb("wrapped", [P, GROUP_CHUNKS], i32)
        row_index = [sb(f"row_index{a}", [P, GROUP_CHUNKS], u32) for a in range(2)]
        db = sb("db", [DENSE, BATCH + HID])
        w = sb("w", [P, WEIGHTS])
        wp = sb("wp", [PAIR_ROWS, PART, T1])
        hidden = sb("hidden", [P, HH, BATCH])
        bottom = sb("bottom", [EMB, BATCH])
        rows = [sb(f"rows{a}", [P, GROUP_CHUNKS, EMB]) for a in range(2)]
        fields = [sb(f"fields{a}", [EMB, GROUP, SLOT]) for a in range(2)]
        pairs = [sb(f"pairs{a}", [PAIR_ROWS, PART, GROUP]) for a in range(2)]
        top1 = sb("top1", [T1, GROUP])
        top2 = sb("top2", [T2, GROUP])
        probs = sb("probs", [1, BATCH])
        warm = sb("warm", [1, 1])

        index_loaded, dense_loaded, weights_loaded, pair_weights_loaded, stored = map(
            sem, ["index_loaded", "dense_loaded", "weights_loaded", "pair_weights_loaded", "stored"])
        gathered = [[sem(f"gathered{a}_{c}") for c in range(GROUP_CHUNKS)] for a in range(2)]
        wrap_done, wrapped_done = sem("wrap_done"), sem("wrapped_done")
        queued = sem("queued")
        index_ready = sem("index_ready")
        hidden_made, hidden_ready = sem("hidden_made"), sem("hidden_ready")
        bottom_made, bottom_ready = sem("bottom_made"), sem("bottom_ready")
        cleared = sem("cleared")
        transposed = sem("transposed")
        fields_ready = sem("fields_ready")
        multiplied = sem("multiplied")
        taken_dve = [sem(f"taken_dve{k}") for k in range(2)]
        taken_act = [sem(f"taken_act{k}") for k in range(2)]
        group_used = [sem(f"group_used{a}") for a in range(2)]
        top1_ready, top2_made, top2_ready = sem("top1_ready"), sem("top2_made"), sem("top2_ready")
        logits_made, probs_ready = sem("logits_made"), sem("probs_ready")
        warmed = sem("warmed")

        def rounds(eng, body):
            with eng.Fori(0, ROUNDS - 1) as turn:
                body(turn, False)
            body(ROUNDS - 1, True)

        def bank_of(a, m):
            n = a * NB + m
            return n % 2, n // 2

        USES = NB

        def take_pairs(copy, k, a, m, quadrants):
            _, q0, q1 = BATCHES[m]
            src = products[k][:, 0:(q1 - q0) * QUAD * SPARSE].rearrange(
                "p (q s g) -> p s g q", s=QUAD, g=SPARSE)
            dst = pairs[a][:, :, :].rearrange("p g (q s) -> p s g q", s=QUAD)
            for s in quadrants:
                for j in range(SPLIT):
                    g0, g1 = j * PART, min((j + 1) * PART, SPARSE)
                    last = copy(dst[SLOT * j:SLOT * (j + 1), s, 0:g1 - g0, q0:q1],
                                src[SLOT * s:SLOT * (s + 1), s, g0:g1, :])
            return last

        block = ctx.enter_context(nc.Block())

        @block.sync
        def _(sp):
            sp.dma_start(raw[:, :], index_base).then_inc(index_loaded, 16)
            sp.dma_start(w[:, :], weights).then_inc(weights_loaded, 16)
            sp.dma_start(wp[:, :, :], pair_weights).then_inc(pair_weights_loaded, 16)
            sp.wait_ge(probs_ready, GROUPS)
            sp.dma_start(out, probs[:, :]).then_inc(stored, 16)
            sp.wait_ge(stored, 16)

        @block.gpsimd
        def _(pool):
            def turn(t, last):
                for a in range(2):
                    pool.wait_ge(index_ready, 2 * t + a + 1)
                    pool.sem_inc(queued, 1)
                    for c in range(GROUP_CHUNKS):
                        nc.gpsimd.indirect_dma_start(
                            rows[a][:, c, :], None, table,
                            bass.IndirectOffsetOnAxis(row_index[a][:, c:c + 1], 0)
                        ).then_inc(gathered[a][c], 16)
            rounds(pool, turn)

        @block.vector
        def _(dve):
            def make_indices(group, a):
                given = raw[:, bass.ds(group * GROUP_CHUNKS, GROUP_CHUNKS)]
                nc.vector.tensor_scalar(wrap[:, :], given, 0.0, float(VOCAB),
                                        ALU.is_lt, ALU.mult).then_inc(wrap_done, 1)
                dve.wait_ge(wrap_done, group + 1)
                nc.vector.scalar_tensor_tensor(wrapped[:, :], given, float(VOCAB - 1), wrap[:, :],
                                               ALU.min, ALU.add).then_inc(wrapped_done, 1)
                dve.wait_ge(wrapped_done, group + 1)
                nc.vector.scalar_tensor_tensor(row_index[a][:, :], wrapped[:, :], 0.0,
                                               raw[:, GROUPS * GROUP_CHUNKS:], ALU.max,
                                               ALU.add).then_inc(index_ready, 1)

            dve.wait_ge(index_loaded, 16)
            make_indices(0, 0)
            make_indices(1, 1)
            nc.vector.memset(fields[0][:, :, :], 0.0).then_inc(cleared, 1)
            nc.vector.memset(fields[1][:, :, :], 0.0).then_inc(cleared, 1)
            dve.wait_ge(cleared, 2)
            dve.wait_ge(bottom_ready, 1)

            def turn(t, last):
                for a in range(2):
                    group = 2 * t + a
                    nc.vector.tensor_copy(fields[a][:, :, 0], bottom[:, bass.ds(group * GROUP, GROUP)])
                    m = 0
                    for u, (c0, c1) in enumerate(UNITS):
                        dve.wait_ge(transposed, NU * group + u + 1)
                        src = rows_T[(a * NU + u) % 2]
                        for col, n, b, f, nf in evacuation_pieces(c0, c1):
                            ins = nc.vector.tensor_copy(
                                fields[a][:, b:b + n, 1 + f:1 + f + nf],
                                src[:, col:col + n * nf].rearrange("p (n f) -> p n f", f=nf))
                        ins.then_inc(fields_ready, 1)
                        if u == NU - 1 and not last:
                            make_indices(group + 2, a)
                        while m < NB and BATCHES[m][0] == u:
                            k, before = bank_of(a, m)
                            dve.wait_ge(multiplied, NB * group + m + 1)
                            take_pairs(nc.vector.tensor_copy, k, a, m, (0, 1)).then_inc(taken_dve[k], 1)
                            m += 1
            rounds(dve, turn)

        @block.scalar
        def _(act):
            act.dma_start(db[:, :], dense_bw1).then_inc(dense_loaded, 16)
            nc.scalar.activation(warm[:, :], nc.const_aps.tensor(0.0, (1, 1), fp32),
                                 ACT.Sigmoid).then_inc(warmed, 1)
            act.wait_ge(weights_loaded, 16)
            for h in range(HH):
                act.wait_ge(hidden_made, h + 1)
                nc.scalar.activation(hidden[:, h, :], rows_T[h][:, 0:BATCH], ACT.Relu,
                                     bias=w[:, BB1 + h:BB1 + h + 1]).then_inc(hidden_ready, 1)
            act.wait_ge(bottom_made, 1)
            nc.scalar.activation(bottom[:, :], products[0][:, 0:BATCH], ACT.Relu,
                                 bias=w[:, BB2:BB2 + 1]).then_inc(bottom_ready, 1)

            def turn(t, last):
                for a in range(2):
                    group = 2 * t + a
                    for m in range(NB):
                        k, before = bank_of(a, m)
                        act.wait_ge(multiplied, NB * group + m + 1)
                        take_pairs(nc.scalar.copy, k, a, m, (2, 3)).then_inc(taken_act[k], 1)
                    act.wait_ge(group_used[a], t + 1)
                    nc.scalar.activation(top1[:, :], top1_ps[:, 0:GROUP], ACT.Relu,
                                         bias=w[:, TB1:TB1 + 1]).then_inc(top1_ready, 1)
                    act.wait_ge(top2_made, group + 1)
                    nc.scalar.activation(top2[:, :], top2_ps[0:T2, 0:GROUP], ACT.Relu,
                                         bias=w[0:T2, TB2:TB2 + 1]).then_inc(top2_ready, 1)
                    act.wait_ge(logits_made, group + 1)
                    nc.scalar.activation(probs[:, bass.ds(group * GROUP, GROUP)], logit_ps[0:1, 0:GROUP],
                                         ACT.Sigmoid, bias=w[0:1, TB3:TB3 + 1]).then_inc(probs_ready, 1)
            rounds(act, turn)

        @block.tensor
        def _(pe):
            pe.wait_ge(dense_loaded, 16)
            for h in range(HH):
                nc.tensor.matmul(rows_T[h][:, 0:BATCH], db[:, BATCH + h * P:BATCH + (h + 1) * P],
                                 db[:, 0:BATCH], start=True, stop=True).then_inc(hidden_made, 1)
            pe.wait_ge(weights_loaded, 16)
            for h in range(HH):
                pe.wait_ge(hidden_ready, h + 1)
                ins = nc.tensor.matmul(products[0][:, 0:BATCH], w[:, BW2 + h * EMB:BW2 + (h + 1) * EMB],
                                       hidden[:, h, :], start=(h == 0), stop=(h == HH - 1))
            ins.then_inc(bottom_made, 1)
            pe.wait_ge(bottom_ready, 1)
            pe.wait_ge(pair_weights_loaded, 16)

            def turn(t, last):
                for a in range(2):
                    group = 2 * t + a
                    m = 0
                    for u, (c0, c1) in enumerate(UNITS):
                        for c in range(c0, c1):
                            pe.wait_ge(gathered[a][c], 16 * t + 16)
                            ins = nc.tensor.transpose(rows_T[(a * NU + u) % 2][:, (c - c0) * P:(c - c0 + 1) * P],
                                                      rows[a][:, c, :], w[:, IDENT:IDENT + P])
                        ins.then_inc(transposed, 1)
                        pe.wait_ge(fields_ready, NU * group + u + 1)
                        while m < NB and BATCHES[m][0] == u:
                            k, before = bank_of(a, m)
                            if m >= 2:
                                pe.wait_ge(taken_dve[k], USES * t + before)
                                pe.wait_ge(taken_act[k], USES * t + before)
                            _, q0, q1 = BATCHES[m]
                            for q in range(q0, q1):
                                four = fields[a][:, q * QUAD:(q + 1) * QUAD, :]
                                n = QUAD * SPARSE
                                ins = nc.tensor.matmul(products[k][:, (q - q0) * n:(q - q0 + 1) * n],
                                                       four, four[:, :, 1:1 + SPARSE],
                                                       start=True, stop=True)
                            ins.then_inc(multiplied, 1)
                            m += 1
                    nc.tensor.matmul(top1_ps[:, 0:GROUP], w[:, TW1X:TW1X + T1], fields[a][:, :, 0],
                                     start=True, stop=False)
                    for k in range(2):
                        used = max(n // 2 + 1 for n in range(a * NB, (a + 1) * NB) if n % 2 == k)
                        pe.wait_ge(taken_dve[k], USES * t + used)
                        pe.wait_ge(taken_act[k], USES * t + used)
                    for g in range(PART):
                        ins = nc.tensor.matmul(top1_ps[:, 0:GROUP], wp[:, g, :], pairs[a][:, g, :],
                                               start=False, stop=(g == PART - 1))
                    ins.then_inc(group_used[a], 1)
                    pe.wait_ge(top1_ready, group + 1)
                    nc.tensor.matmul(top2_ps[0:T2, 0:GROUP], w[:, TW2:TW2 + T2], top1[:, :],
                                     start=True, stop=True).then_inc(top2_made, 1)
                    pe.wait_ge(weights_loaded, 16)
                    pe.wait_ge(top2_ready, group + 1)
                    nc.tensor.matmul(logit_ps[0:1, 0:GROUP], w[0:T2, TW3:TW3 + 1], top2[:, :],
                                     start=True, stop=True).then_inc(logits_made, 1)
            rounds(pe, turn)


def pair_weight_order():
    import numpy as np
    where = -np.ones((SPLIT, SLOT, PART), np.int64)
    rows, cols = np.triu_indices(SPARSE + 1, k=1)
    for n, (f, g) in enumerate(zip(rows, cols)):
        where[(g - 1) // PART, f, (g - 1) % PART] = EMB + n
    return where.reshape(PAIR_ROWS, PART)


def kernel(r_dense_x, r_sparse_x, L0_rec_emb_tables, L0_rec_bw1, L0_rec_bb1, L0_rec_bw2, L0_rec_bb2,
           L0_rec_tw1, L0_rec_tb1, L0_rec_tw2, L0_rec_tb2, L0_rec_tw3, L0_rec_tb3):
    import numpy as np
    import concourse.bacc as bacc
    from concourse.bass_utils import run_bass_kernel_spmd

    chunks = GROUPS * GROUP_CHUNKS
    index = np.asarray(r_sparse_x).reshape(chunks, P).T
    base = ((np.arange(GROUP_ROWS) % SPARSE) * VOCAB).astype(np.int32).reshape(GROUP_CHUNKS, P).T

    def columns(a, rows=P):
        a = np.asarray(a)
        out = np.zeros((P, a.shape[1]), a.dtype)
        out[:a.shape[0]] = a
        return out

    bw2 = np.asarray(L0_rec_bw2)
    tw1 = np.asarray(L0_rec_tw1)
    weights = np.concatenate([
        np.eye(P, dtype=np.float32), *[bw2[h * P:(h + 1) * P] for h in range(HH)], tw1[:EMB],
        np.asarray(L0_rec_tw2), columns(L0_rec_tw3), np.asarray(L0_rec_bb1).reshape(HH, P).T,
        np.asarray(L0_rec_bb2)[:, None], np.asarray(L0_rec_tb1)[:, None],
        columns(np.asarray(L0_rec_tb2)[:, None]), columns(np.asarray(L0_rec_tb3)[:, None])], axis=1)
    where = pair_weight_order()
    pair_weights = np.zeros((PAIR_ROWS, PART, T1), tw1.dtype)
    pair_weights[where >= 0] = tw1[where[where >= 0]]
    arrays = {
        "index_base": np.ascontiguousarray(np.concatenate([index, base], axis=1)),
        "dense_bw1": np.ascontiguousarray(np.concatenate([np.asarray(r_dense_x).T, np.asarray(L0_rec_bw1)], axis=1)),
        "weights": np.ascontiguousarray(weights),
        "pair_weights": pair_weights,
        "table": np.asarray(L0_rec_emb_tables).reshape(SPARSE * VOCAB, EMB),
    }
    assert weights.shape[1] == WEIGHTS
    nc = bacc.Bacc("TRN2", target_bir_lowering=False, num_devices=1)
    args = [nc.dram_tensor(n, a.shape, mybir.dt.from_np(a.dtype), kind="ExternalInput").ap()
            for n, a in arrays.items()]
    out = nc.dram_tensor("out", (1, BATCH), mybir.dt.float32, kind="ExternalOutput").ap()
    dlrm(nc, *args, out)
    got = run_bass_kernel_spmd(nc, [arrays], core_ids=[0])
    return got.results[0]["out"].reshape(BATCH, 1)
```

```python
import concourse.bass as bass
from concourse import mybir
from contextlib import ExitStack
from math import lcm

P = 128
BATCH = 512
SPARSE = 26
VOCAB = 12500
EMB = 128
DENSE = 13
HID = 256
T1, T2 = 128, 64
HH = HID // P

SLOT = 32
QUAD = P // SLOT
GROUP_ROWS = lcm(SPARSE, P)
GROUP_CHUNKS = GROUP_ROWS // P
GROUP = GROUP_ROWS // SPARSE
GROUPS = BATCH // GROUP
ROUNDS = GROUPS // 2

BANK = 512
UNIT_CHUNKS = BANK // P
UNITS = [(c, min(c + UNIT_CHUNKS, GROUP_CHUNKS)) for c in range(0, GROUP_CHUNKS, UNIT_CHUNKS)]

SPLIT = 4
PART = -(-SPARSE // SPLIT)
PAIR_ROWS = SLOT * SPLIT

BATCH_QUADS = 4


def quad_batches():
    out, at = [], 0
    quads = GROUP // QUAD
    for u, (_, c1) in enumerate(UNITS):
        ready = c1 * P // SPARSE // QUAD
        while ready - at >= BATCH_QUADS or (u >= len(UNITS) - 2 and ready > at):
            end = min(at + BATCH_QUADS, ready)
            out.append((u, at, end))
            at = end
    assert at == quads
    return out


BATCHES = quad_batches()
PRODUCT_BANKS = 3
USES = [len(range(k, len(BATCHES), PRODUCT_BANKS)) for k in range(PRODUCT_BANKS)]
TURN = 2 * GROUP


def evacuation_pieces(c0, c1):
    row, end, out = c0 * P, c1 * P, []
    while row < end:
        b, f = divmod(row, SPARSE)
        if f or end - row < SPARSE:
            n = min(SPARSE - f, end - row)
            out.append((row - c0 * P, 1, b, f, n))
            row += n
        else:
            k = (end - row) // SPARSE
            out.append((row - c0 * P, k, b, 0, SPARSE))
            row += k * SPARSE
    return out


IDENT = 0
BW2 = IDENT + P
TW1X = BW2 + HH * EMB
TW2 = TW1X + T1
TW3 = TW2 + T2
BB1 = TW3 + 1
BB2 = BB1 + HH
TB1 = BB2 + 1
TB2 = TB1 + 1
TB3 = TB2 + 1
WEIGHTS = TB3 + 1


def dlrm(nc, index_base, dense_bw1, weights, pair_weights, table, out):
    fp32, i32, u32 = mybir.dt.float32, mybir.dt.int32, mybir.dt.uint32
    ALU = mybir.AluOpType
    ACT = mybir.ActivationFunctionType
    NB, NU = len(BATCHES), len(UNITS)

    ctx = ExitStack()
    with ctx:
        def sb(name, shape, dt=fp32):
            return ctx.enter_context(nc.sbuf_tensor(name, shape, dt))

        def sem(name):
            return ctx.enter_context(nc.semaphore(name))

        banks = [ctx.enter_context(nc.psum_tensor(f"bank{i}", [P, BANK], fp32)) for i in range(8)]
        rows_T = banks[0:2]
        products = banks[2:2 + PRODUCT_BANKS]
        top1_ps, top2_ps, logit_ps = banks[5:8]

        raw = sb("raw", [P, GROUPS * GROUP_CHUNKS + GROUP_CHUNKS], i32)
        wrap = sb("wrap", [P, GROUP_CHUNKS], i32)
        wrapped = sb("wrapped", [P, GROUP_CHUNKS], i32)
        row_index = [sb(f"row_index{a}", [P, GROUP_CHUNKS], u32) for a in range(2)]
        db = sb("db", [DENSE, BATCH + HID])
        w = sb("w", [P, WEIGHTS])
        wp = sb("wp", [PAIR_ROWS, PART, T1])
        hidden = sb("hidden", [P, HH, BATCH])
        bottom = sb("bottom", [EMB, BATCH])
        rows = [sb(f"rows{a}", [P, GROUP_CHUNKS, EMB]) for a in range(2)]
        fields = [sb(f"fields{a}", [EMB, GROUP, SLOT]) for a in range(2)]
        pairs = sb("pairs", [PAIR_ROWS, PART, TURN])
        top1 = sb("top1", [T1, TURN])
        top2 = sb("top2", [T2, TURN])
        probs = sb("probs", [1, BATCH])
        warm = sb("warm", [1, 1])

        index_loaded, dense_loaded, weights_loaded, pair_weights_loaded, stored = map(
            sem, ["index_loaded", "dense_loaded", "weights_loaded", "pair_weights_loaded", "stored"])
        gathered = [[sem(f"gathered{a}_{c}") for c in range(GROUP_CHUNKS)] for a in range(2)]
        wrap_done, wrapped_done = sem("wrap_done"), sem("wrapped_done")
        queued = sem("queued")
        index_ready = sem("index_ready")
        hidden_made, hidden_ready = sem("hidden_made"), sem("hidden_ready")
        bottom_made, bottom_ready = sem("bottom_made"), sem("bottom_ready")
        cleared = sem("cleared")
        transposed = sem("transposed")
        fields_ready = sem("fields_ready")
        multiplied = sem("multiplied")
        taken_dve = [sem(f"taken_dve{k}") for k in range(PRODUCT_BANKS)]
        taken_act = [sem(f"taken_act{k}") for k in range(PRODUCT_BANKS)]
        top1_made, top1_ready = sem("top1_made"), sem("top1_ready")
        top2_made, top2_ready = sem("top2_made"), sem("top2_ready")
        logits_made, probs_ready = sem("logits_made"), sem("probs_ready")
        warmed = sem("warmed")

        def rounds(eng, body):
            with eng.Fori(0, ROUNDS - 1) as turn:
                body(turn, False)
            body(ROUNDS - 1, True)

        def group_order(a, last, unit_in, unit_on):
            final = last and a == 1
            for u in range(NU):
                if u + 1 < NU and not final:
                    unit_in(a, u + 1, 0)
                unit_on(a, u)
                if u + 1 < NU and final:
                    unit_in(a, u + 1, 0)
            if not final:
                unit_in(1 - a, 0, a)

        def take_pairs(copy, a, m, quadrants):
            _, q0, q1 = BATCHES[m]
            src = products[m % PRODUCT_BANKS][:, 0:(q1 - q0) * QUAD * SPARSE].rearrange(
                "p (q s g) -> p s g q", s=QUAD, g=SPARSE)
            dst = pairs[:, :, a * GROUP:(a + 1) * GROUP].rearrange("p g (q s) -> p s g q", s=QUAD)
            for s in quadrants:
                for j in range(SPLIT):
                    g0, g1 = j * PART, min((j + 1) * PART, SPARSE)
                    last = copy(dst[SLOT * j:SLOT * (j + 1), s, 0:g1 - g0, q0:q1],
                                src[SLOT * s:SLOT * (s + 1), s, g0:g1, :])
            return last

        block = ctx.enter_context(nc.Block())

        @block.sync
        def _(sp):
            sp.dma_start(raw[:, :], index_base).then_inc(index_loaded, 16)
            sp.dma_start(w[:, :], weights).then_inc(weights_loaded, 16)
            sp.dma_start(wp[:, :, :], pair_weights).then_inc(pair_weights_loaded, 16)
            sp.wait_ge(probs_ready, ROUNDS)
            sp.dma_start(out, probs[:, :]).then_inc(stored, 16)
            sp.wait_ge(stored, 16)

        @block.gpsimd
        def _(pool):
            def turn(t, last):
                for a in range(2):
                    pool.wait_ge(index_ready, 2 * t + a + 1)
                    pool.sem_inc(queued, 1)
                    for c in range(GROUP_CHUNKS):
                        nc.gpsimd.indirect_dma_start(
                            rows[a][:, c, :], None, table,
                            bass.IndirectOffsetOnAxis(row_index[a][:, c:c + 1], 0)
                        ).then_inc(gathered[a][c], 16)
            rounds(pool, turn)

        @block.vector
        def _(dve):
            def make_indices(group, a):
                given = raw[:, bass.ds(group * GROUP_CHUNKS, GROUP_CHUNKS)]
                nc.vector.tensor_scalar(wrap[:, :], given, 0.0, float(VOCAB),
                                        ALU.is_lt, ALU.mult).then_inc(wrap_done, 1)
                dve.wait_ge(wrap_done, group + 1)
                nc.vector.scalar_tensor_tensor(wrapped[:, :], given, float(VOCAB - 1), wrap[:, :],
                                               ALU.min, ALU.add).then_inc(wrapped_done, 1)
                dve.wait_ge(wrapped_done, group + 1)
                nc.vector.scalar_tensor_tensor(row_index[a][:, :], wrapped[:, :], 0.0,
                                               raw[:, GROUPS * GROUP_CHUNKS:], ALU.max,
                                               ALU.add).then_inc(index_ready, 1)

            dve.wait_ge(index_loaded, 16)
            make_indices(0, 0)
            make_indices(1, 1)
            for a in range(2):
                nc.vector.memset(fields[a][:, :, SPARSE + 1:SLOT], 0.0)
            nc.vector.memset(pairs[SLOT * (SPLIT - 1):, SPARSE - PART * (SPLIT - 1):, :],
                             0.0).then_inc(cleared, 1)
            for k in range(PRODUCT_BANKS):
                dve.sem_inc(taken_dve[k], 1)
            dve.wait_ge(bottom_ready, 1)

            def fields_in(a, u, t_next, t):
                group = 2 * (t + t_next) + a
                if u == 0:
                    nc.vector.tensor_copy(fields[a][:, :, 0], bottom[:, bass.ds(group * GROUP, GROUP)])
                dve.wait_ge(transposed, NU * group + u + 1)
                c0, c1 = UNITS[u]
                for col, n, b, f, nf in evacuation_pieces(c0, c1):
                    ins = nc.vector.tensor_copy(
                        fields[a][:, b:b + n, 1 + f:1 + f + nf],
                        rows_T[(a * NU + u) % 2][:, col:col + n * nf].rearrange("p (n f) -> p n f", f=nf))
                ins.then_inc(fields_ready, 1)

            fields_in(0, 0, 0, 0)

            def turn(t, last):
                def unit_in(a, u, t_next):
                    fields_in(a, u, t_next, t)
                    if u == NU - 1 and not last:
                        make_indices(2 * t + a + 2, a)

                def unit_on(a, u):
                    for m in range(NB):
                        if BATCHES[m][0] == u:
                            dve.wait_ge(multiplied, NB * (2 * t + a) + m + 1)
                            take_pairs(nc.vector.tensor_copy, a, m, (0, 1)).then_inc(
                                taken_dve[m % PRODUCT_BANKS], 1)

                for a in range(2):
                    group_order(a, last, unit_in, unit_on)
            rounds(dve, turn)

        @block.scalar
        def _(act):
            act.dma_start(db[:, :], dense_bw1).then_inc(dense_loaded, 16)
            nc.scalar.activation(warm[:, :], nc.const_aps.tensor(0.0, (1, 1), fp32),
                                 ACT.Sigmoid).then_inc(warmed, 1)
            for k in range(PRODUCT_BANKS):
                act.sem_inc(taken_act[k], 1)
            act.wait_ge(weights_loaded, 16)
            for h in range(HH):
                act.wait_ge(hidden_made, h + 1)
                nc.scalar.activation(hidden[:, h, :], rows_T[h][:, 0:BATCH], ACT.Relu,
                                     bias=w[:, BB1 + h:BB1 + h + 1]).then_inc(hidden_ready, 1)
            act.wait_ge(bottom_made, 1)
            nc.scalar.activation(bottom[:, :], products[0][:, 0:BATCH], ACT.Relu,
                                 bias=w[:, BB2:BB2 + 1]).then_inc(bottom_ready, 1)

            def turn(t, last):
                for a in range(2):
                    for m in range(NB):
                        act.wait_ge(multiplied, NB * (2 * t + a) + m + 1)
                        take_pairs(nc.scalar.copy, a, m, (2, 3)).then_inc(taken_act[m % PRODUCT_BANKS], 1)
                act.wait_ge(top1_made, t + 1)
                nc.scalar.activation(top1[:, :], top1_ps[:, 0:TURN], ACT.Relu,
                                     bias=w[:, TB1:TB1 + 1]).then_inc(top1_ready, 1)
                act.wait_ge(top2_made, t + 1)
                nc.scalar.activation(top2[:, :], top2_ps[0:T2, 0:TURN], ACT.Relu,
                                     bias=w[0:T2, TB2:TB2 + 1]).then_inc(top2_ready, 1)
                act.wait_ge(logits_made, t + 1)
                nc.scalar.activation(probs[:, bass.ds(t * TURN, TURN)], logit_ps[0:1, 0:TURN],
                                     ACT.Sigmoid, bias=w[0:1, TB3:TB3 + 1]).then_inc(probs_ready, 1)
            rounds(act, turn)

        @block.tensor
        def _(pe):
            pe.wait_ge(dense_loaded, 16)
            for h in range(HH):
                nc.tensor.matmul(rows_T[h][:, 0:BATCH], db[:, BATCH + h * P:BATCH + (h + 1) * P],
                                 db[:, 0:BATCH], start=True, stop=True).then_inc(hidden_made, 1)
            pe.wait_ge(weights_loaded, 16)
            for h in range(HH):
                pe.wait_ge(hidden_ready, h + 1)
                ins = nc.tensor.matmul(products[0][:, 0:BATCH], w[:, BW2 + h * EMB:BW2 + (h + 1) * EMB],
                                       hidden[:, h, :], start=(h == 0), stop=(h == HH - 1))
            ins.then_inc(bottom_made, 1)

            def transposes(a, u, t_next, t):
                c0, c1 = UNITS[u]
                for c in range(c0, c1):
                    pe.wait_ge(gathered[a][c], 16 * (t + t_next) + 16)
                    ins = nc.tensor.transpose(rows_T[(a * NU + u) % 2][:, (c - c0) * P:(c - c0 + 1) * P],
                                              rows[a][:, c, :], w[:, IDENT:IDENT + P])
                ins.then_inc(transposed, 1)

            transposes(0, 0, 0, 0)
            pe.wait_ge(bottom_ready, 1)
            pe.wait_ge(pair_weights_loaded, 16)

            def turn(t, last):
                def unit_on(a, u):
                    group = 2 * t + a
                    pe.wait_ge(fields_ready, NU * group + u + 1)
                    for m in range(NB):
                        if BATCHES[m][0] != u:
                            continue
                        k = m % PRODUCT_BANKS
                        taken = USES[k] * group + m // PRODUCT_BANKS + 1
                        pe.wait_ge(taken_dve[k], taken)
                        pe.wait_ge(taken_act[k], taken)
                        _, q0, q1 = BATCHES[m]
                        n = QUAD * SPARSE
                        for q in range(q0, q1):
                            four = fields[a][:, q * QUAD:(q + 1) * QUAD, :]
                            ins = nc.tensor.matmul(products[k][:, (q - q0) * n:(q - q0 + 1) * n],
                                                   four, four[:, :, 1:1 + SPARSE], start=True, stop=True)
                        ins.then_inc(multiplied, 1)

                for a in range(2):
                    group_order(a, last, lambda a, u, t_next: transposes(a, u, t_next, t), unit_on)

                nc.tensor.matmul(top1_ps[:, 0:TURN], w[:, TW1X:TW1X + T1],
                                 bottom[:, bass.ds(t * TURN, TURN)], start=True, stop=False)
                for k in range(PRODUCT_BANKS):
                    pe.wait_ge(taken_dve[k], USES[k] * 2 * (t + 1) + 1)
                    pe.wait_ge(taken_act[k], USES[k] * 2 * (t + 1) + 1)
                for g in range(PART):
                    ins = nc.tensor.matmul(top1_ps[:, 0:TURN], wp[:, g, :], pairs[:, g, :],
                                           start=False, stop=(g == PART - 1))
                ins.then_inc(top1_made, 1)
                pe.wait_ge(top1_ready, t + 1)
                nc.tensor.matmul(top2_ps[0:T2, 0:TURN], w[:, TW2:TW2 + T2], top1[:, :],
                                 start=True, stop=True).then_inc(top2_made, 1)
                pe.wait_ge(weights_loaded, 16)
                pe.wait_ge(top2_ready, t + 1)
                nc.tensor.matmul(logit_ps[0:1, 0:TURN], w[0:T2, TW3:TW3 + 1], top2[:, :],
                                 start=True, stop=True).then_inc(logits_made, 1)
            rounds(pe, turn)


def pair_weight_order():
    import numpy as np
    where = -np.ones((SPLIT, SLOT, PART), np.int64)
    rows, cols = np.triu_indices(SPARSE + 1, k=1)
    for n, (f, g) in enumerate(zip(rows, cols)):
        where[(g - 1) // PART, f, (g - 1) % PART] = EMB + n
    return where.reshape(PAIR_ROWS, PART)


def kernel(r_dense_x, r_sparse_x, L0_rec_emb_tables, L0_rec_bw1, L0_rec_bb1, L0_rec_bw2, L0_rec_bb2,
           L0_rec_tw1, L0_rec_tb1, L0_rec_tw2, L0_rec_tb2, L0_rec_tw3, L0_rec_tb3):
    import numpy as np
    import concourse.bacc as bacc
    from concourse.bass_utils import run_bass_kernel_spmd

    chunks = GROUPS * GROUP_CHUNKS
    index = np.asarray(r_sparse_x).reshape(chunks, P).T
    base = ((np.arange(GROUP_ROWS) % SPARSE) * VOCAB).astype(np.int32).reshape(GROUP_CHUNKS, P).T

    def columns(a, rows=P):
        a = np.asarray(a)
        out = np.zeros((P, a.shape[1]), a.dtype)
        out[:a.shape[0]] = a
        return out

    bw2 = np.asarray(L0_rec_bw2)
    tw1 = np.asarray(L0_rec_tw1)
    weights = np.concatenate([
        np.eye(P, dtype=np.float32), *[bw2[h * P:(h + 1) * P] for h in range(HH)], tw1[:EMB],
        np.asarray(L0_rec_tw2), columns(L0_rec_tw3), np.asarray(L0_rec_bb1).reshape(HH, P).T,
        np.asarray(L0_rec_bb2)[:, None], np.asarray(L0_rec_tb1)[:, None],
        columns(np.asarray(L0_rec_tb2)[:, None]), columns(np.asarray(L0_rec_tb3)[:, None])], axis=1)
    where = pair_weight_order()
    pair_weights = np.zeros((PAIR_ROWS, PART, T1), tw1.dtype)
    pair_weights[where >= 0] = tw1[where[where >= 0]]
    arrays = {
        "index_base": np.ascontiguousarray(np.concatenate([index, base], axis=1)),
        "dense_bw1": np.ascontiguousarray(np.concatenate([np.asarray(r_dense_x).T, np.asarray(L0_rec_bw1)], axis=1)),
        "weights": np.ascontiguousarray(weights),
        "pair_weights": pair_weights,
        "table": np.asarray(L0_rec_emb_tables).reshape(SPARSE * VOCAB, EMB),
    }
    assert weights.shape[1] == WEIGHTS
    nc = bacc.Bacc("TRN2", target_bir_lowering=False, num_devices=1)
    args = [nc.dram_tensor(n, a.shape, mybir.dt.from_np(a.dtype), kind="ExternalInput").ap()
            for n, a in arrays.items()]
    out = nc.dram_tensor("out", (1, BATCH), mybir.dt.float32, kind="ExternalOutput").ap()
    dlrm(nc, *args, out)
    got = run_bass_kernel_spmd(nc, [arrays], core_ids=[0])
    return got.results[0]["out"].reshape(BATCH, 1)
```
